# Optimizing a Trainium2 kernel written in Bass

```python
import numpy as np
import jax
import jax.numpy as jnp

def _softmax(x, axis=-1):
    return jax.nn.softmax(x, axis=axis)
def _gelu(x):
    return jax.nn.gelu(x, approximate=True)
def _silu(x):
    return jax.nn.silu(x)
def _sigmoid(x):
    return jax.nn.sigmoid(x)
def _layernorm(x, axis=-1, eps=1e-5):
    m = jnp.mean(x, axis=axis, keepdims=True)
    v = jnp.var(x, axis=axis, keepdims=True)
    return (x - m) / jnp.sqrt(v + eps)
def _scatter_add(tgt, idx, src, axis=0):
    return tgt.at[idx].add(src)
def _segment_sum(src, seg, n):
    return jax.ops.segment_sum(src, seg, n)

kernel_name = 'mk_conv_preact_d2_conv_nchw512_361ed1'

def setup_inputs(seed: int = 0):
    np.random.seed(seed)
    _w = jnp.asarray
    def _rec_inputs():
        import jax
        import jax.numpy as jnp
        _gk = jax.random.key(seed)
        x = -0.0002928 + 1 * jax.random.normal(jax.random.fold_in(_gk, 1), (8, 512, 32, 32), jnp.float32)
        return x
    x = _rec_inputs()
    def _L0_conv_setup():
        import jax, jax.numpy as jnp
        import numpy as np
        B, C, H, W = (8, 512, 32, 32)
        NUM_HEADS = 8
        HEAD_SIZE = C // NUM_HEADS
        key = jax.random.key(seed)
        k_x, k_wqkv, k_bqkv, k_wo, k_bo = jax.random.split(key, 5)
        s = 1.0 / np.sqrt(C)
        x = jax.random.normal(k_x, (B, C, H, W), dtype=jnp.float32)
        Wqkv = jax.random.uniform(k_wqkv, (C, 3 * C), jnp.float32, -s, s)
        bqkv = jax.random.uniform(k_bqkv, (3 * C,), jnp.float32, -s, s)
        Wout = jax.random.uniform(k_wo, (C, C), jnp.float32, -s, s)
        bout = jax.random.uniform(k_bo, (C,), jnp.float32, -s, s)
        return {'x': x, 'Wqkv': Wqkv, 'bqkv': bqkv, 'Wout': Wout, 'bout': bout}
    _L0_conv_all = _L0_conv_setup()
    _L0_conv_in = {k: v for k, v in _L0_conv_all.items() if k in ('Wqkv', 'bqkv', 'Wout', 'bout', )}
    del _L0_conv_all

    def _L1_conv_setup():
        import jax, jax.numpy as jnp
        import numpy as np
        DIM = 512
        HEADS = 8
        DIM_HEAD = 64
        G = 8
        OFF_DIMS = 64
        DS = 4
        OFF_SCALE = 4.0
        SCALE = DIM_HEAD ** (-0.5)

        def _grid_sample(img, grid):
            N, C, H, W = img.shape
            Hg, Wg = grid.shape[1:3]
            ix = ((grid[..., 0] + 1.0) * W - 1.0) * 0.5
            iy = ((grid[..., 1] + 1.0) * H - 1.0) * 0.5
            ix0 = jnp.floor(ix)
            iy0 = jnp.floor(iy)
            flat = img.reshape(N, C, H * W)

            def gather(xa, ya):
                valid = ((xa >= 0) & (xa <= W - 1) & (ya >= 0) & (ya <= H - 1)).astype(img.dtype)
                idx = (jnp.clip(ya, 0, W - 1) * W + jnp.clip(xa, 0, W - 1)).astype(jnp.int32).reshape(N, 1, Hg * Wg)
                vals = jnp.take_along_axis(flat, jnp.broadcast_to(idx, (N, C, Hg * Wg)), axis=2).reshape(N, C, Hg, Wg)
                return vals * valid[:, None, :, :]
            wx1 = (ix - ix0)[:, None]
            wy1 = (iy - iy0)[:, None]
            wx0 = 1.0 - wx1
            wy0 = 1.0 - wy1
            return gather(ix0, iy0) * wx0 * wy0 + gather(ix0 + 1.0, iy0) * wx1 * wy0 + gather(ix0, iy0 + 1.0) * wx0 * wy1 + gather(ix0 + 1.0, iy0 + 1.0) * wx1 * wy1

        def _forward(x, ln_w, ln_b, wq, wk, wv, w_out, b_out, off_dw_w, off_dw_b, off_pw_w, cpb_w1, cpb_b1, cpb_w2, cpb_b2, cpb_w3, cpb_b3):
            b, c, Hf, Wf = x.shape
            mu = x.mean(axis=1, keepdims=True)
            var = ((x - mu) ** 2).mean(axis=1, keepdims=True)
            xn = (x - mu) / jnp.sqrt(var + 1e-06) * ln_w[None, :, None, None] + ln_b[None, :, None, None]
            xp = xn.reshape(b, c, 4, 8, 4, 8).transpose(2, 4, 0, 1, 3, 5).reshape(16 * b, c, 8, 8)
            B, C, H, W = xp.shape
            xg = xp.reshape(B, G, OFF_DIMS, H, W)
            q = jnp.einsum('bgihw,goi->bgohw', xg, wq)
            gq = q.reshape(B * G, OFF_DIMS, H, W)
            t = jax.lax.conv_general_dilated(gq, off_dw_w, (DS, DS), [(1, 1), (1, 1)], dimension_numbers=('NCHW', 'OIHW', 'NCHW'), feature_group_count=OFF_DIMS)
            t = jax.nn.gelu(t + off_dw_b[None, :, None, None], approximate=False)
            off = jnp.tanh(jnp.einsum('bchw,oc->bohw', t, off_pw_w)) * OFF_SCALE
            Hp, Wp = off.shape[-2:]
            gx, gy = jnp.meshgrid(jnp.arange(Wp, dtype=x.dtype), jnp.arange(Hp, dtype=x.dtype), indexing='xy')
            vx = gx[None] + off[:, 0]
            vy = gy[None] + off[:, 1]
            vgrid = jnp.stack([2.0 * vx / max(Hp - 1, 1) - 1.0, 2.0 * vy / max(Wp - 1, 1) - 1.0], axis=-1)
            kv = _grid_sample(xp.reshape(B * G, OFF_DIMS, H, W), vgrid).reshape(B, G, OFF_DIMS, Hp, Wp)
            k = jnp.einsum('bgihw,goi->bgohw', kv, wk).reshape(B, HEADS, DIM_HEAD, Hp * Wp)
            v = jnp.einsum('bgihw,goi->bgohw', kv, wv).reshape(B, HEADS, DIM_HEAD, Hp * Wp)
            qh = (q * SCALE).reshape(B, HEADS, DIM_HEAD, H * W)
            sim = jnp.einsum('bhdi,bhdj->bhij', qh, k)
            gxq, gyq = jnp.meshgrid(jnp.arange(W, dtype=x.dtype), jnp.arange(H, dtype=x.dtype), indexing='xy')
            qgrid = jnp.stack([2.0 * gxq / max(H - 1, 1) - 1.0, 2.0 * gyq / max(W - 1, 1) - 1.0], axis=-1).reshape(H * W, 2)
            kvgrid = vgrid.reshape(B * G, Hp * Wp, 2)
            pos = qgrid[None, :, None, :] - kvgrid[:, None, :, :]
            bias = jnp.sign(pos) * jnp.log1p(jnp.abs(pos))
            bias = jax.nn.relu(bias @ cpb_w1.T + cpb_b1)
            bias = jax.nn.relu(bias @ cpb_w2.T + cpb_b2)
            bias = bias @ cpb_w3.T + cpb_b3
            sim = sim + bias.reshape(B, HEADS, H * W, Hp * Wp)
            attn = jax.nn.softmax(sim, axis=-1)
            out = jnp.einsum('bhij,bhdj->bhdi', attn, v).reshape(B, DIM, H, W)
            out = jnp.einsum('bchw,oc->bohw', out, w_out) + b_out[None, :, None, None]
            return out.reshape(4, 4, b, c, 8, 8).transpose(2, 3, 0, 4, 1, 5).reshape(b, c, Hf, Wf)
        key = jax.random.key(seed)
        ks = jax.random.split(key, 10)
        s = 0.05
        f32 = jnp.float32
        return {'x': jax.random.normal(ks[0], (64, 512, 32, 32), f32), 'ln_w': jnp.ones((512,), f32), 'ln_b': jnp.zeros((512,), f32), 'wq': jax.random.normal(ks[1], (8, 64, 64), f32) * s, 'wk': jax.random.normal(ks[2], (8, 64, 64), f32) * s, 'wv': jax.random.normal(ks[3], (8, 64, 64), f32) * s, 'w_out': jax.random.normal(ks[4], (512, 512), f32) * s, 'b_out': jnp.zeros((512,), f32), 'off_dw_w': jax.random.normal(ks[5], (64, 1, 6, 6), f32) * s, 'off_dw_b': jnp.zeros((64,), f32), 'off_pw_w': jax.random.normal(ks[6], (2, 64), f32) * s, 'cpb_w1': jax.random.normal(ks[7], (128, 2), f32) * s, 'cpb_b1': jnp.zeros((128,), f32), 'cpb_w2': jax.random.normal(ks[8], (128, 128), f32) * s, 'cpb_b2': jnp.zeros((128,), f32), 'cpb_w3': jax.random.normal(ks[9], (1, 128), f32) * s, 'cpb_b3': jnp.zeros((1,), f32)}
    _L1_conv_all = _L1_conv_setup()
    _L1_conv_in = {k: v for k, v in _L1_conv_all.items() if k in ('ln_w', 'ln_b', 'wq', 'wk', 'wv', 'w_out', 'b_out', 'off_dw_w', 'off_dw_b', 'off_pw_w', 'cpb_w1', 'cpb_b1', 'cpb_w2', 'cpb_b2', 'cpb_w3', 'cpb_b3', )}
    del _L1_conv_all

    return {
        "x": x,
        "L0_conv_Wqkv": _L0_conv_in["Wqkv"],
        "L0_conv_bqkv": _L0_conv_in["bqkv"],
        "L0_conv_Wout": _L0_conv_in["Wout"],
        "L0_conv_bout": _L0_conv_in["bout"],
        "L1_conv_ln_w": _L1_conv_in["ln_w"],
        "L1_conv_ln_b": _L1_conv_in["ln_b"],
        "L1_conv_wq": _L1_conv_in["wq"],
        "L1_conv_wk": _L1_conv_in["wk"],
        "L1_conv_wv": _L1_conv_in["wv"],
        "L1_conv_w_out": _L1_conv_in["w_out"],
        "L1_conv_b_out": _L1_conv_in["b_out"],
        "L1_conv_off_dw_w": _L1_conv_in["off_dw_w"],
        "L1_conv_off_dw_b": _L1_conv_in["off_dw_b"],
        "L1_conv_off_pw_w": _L1_conv_in["off_pw_w"],
        "L1_conv_cpb_w1": _L1_conv_in["cpb_w1"],
        "L1_conv_cpb_b1": _L1_conv_in["cpb_b1"],
        "L1_conv_cpb_w2": _L1_conv_in["cpb_w2"],
        "L1_conv_cpb_b2": _L1_conv_in["cpb_b2"],
        "L1_conv_cpb_w3": _L1_conv_in["cpb_w3"],
        "L1_conv_cpb_b3": _L1_conv_in["cpb_b3"],
    }

def reference(x, L0_conv_Wqkv, L0_conv_bqkv, L0_conv_Wout, L0_conv_bout, L1_conv_ln_w, L1_conv_ln_b, L1_conv_wq, L1_conv_wk, L1_conv_wv, L1_conv_w_out, L1_conv_b_out, L1_conv_off_dw_w, L1_conv_off_dw_b, L1_conv_off_pw_w, L1_conv_cpb_w1, L1_conv_cpb_b1, L1_conv_cpb_w2, L1_conv_cpb_b2, L1_conv_cpb_w3, L1_conv_cpb_b3):
    import jax
    import jax.numpy as jnp
    def _L0_conv_ref(x, Wqkv, bqkv, Wout, bout):
        import jax, jax.numpy as jnp
        import numpy as np
        B, C, H, W = (8, 512, 32, 32)
        NUM_HEADS = 8
        HEAD_SIZE = C // NUM_HEADS
        b, c, h, w = x.shape
        seq = h * w
        xs = x.reshape(b, c, seq).transpose(0, 2, 1)
        qkv = xs @ Wqkv + bqkv
        q, k, v = jnp.split(qkv, 3, axis=-1)

        def heads(t):
            return t.reshape(b, seq, NUM_HEADS, HEAD_SIZE).transpose(0, 2, 1, 3)
        q, k, v = (heads(q), heads(k), heads(v))
        scores = jnp.einsum('bhqd,bhkd->bhqk', q, k) / jnp.sqrt(jnp.asarray(HEAD_SIZE, x.dtype))
        attn = jax.nn.softmax(scores, axis=-1)
        out = jnp.einsum('bhqk,bhkd->bhqd', attn, v)
        out = out.transpose(0, 2, 1, 3).reshape(b, seq, c)
        out = out @ Wout + bout
        return out.transpose(0, 2, 1).reshape(b, c, h, w)

    def _L1_conv_ref(x, ln_w, ln_b, wq, wk, wv, w_out, b_out, off_dw_w, off_dw_b, off_pw_w, cpb_w1, cpb_b1, cpb_w2, cpb_b2, cpb_w3, cpb_b3):
        import jax, jax.numpy as jnp
        import numpy as np
        DIM = 512
        HEADS = 8
        DIM_HEAD = 64
        G = 8
        OFF_DIMS = 64
        DS = 4
        OFF_SCALE = 4.0
        SCALE = DIM_HEAD ** (-0.5)

        def _grid_sample(img, grid):
            N, C, H, W = img.shape
            Hg, Wg = grid.shape[1:3]
            ix = ((grid[..., 0] + 1.0) * W - 1.0) * 0.5
            iy = ((grid[..., 1] + 1.0) * H - 1.0) * 0.5
            ix0 = jnp.floor(ix)
            iy0 = jnp.floor(iy)
            flat = img.reshape(N, C, H * W)

            def gather(xa, ya):
                valid = ((xa >= 0) & (xa <= W - 1) & (ya >= 0) & (ya <= H - 1)).astype(img.dtype)
                idx = (jnp.clip(ya, 0, W - 1) * W + jnp.clip(xa, 0, W - 1)).astype(jnp.int32).reshape(N, 1, Hg * Wg)
                vals = jnp.take_along_axis(flat, jnp.broadcast_to(idx, (N, C, Hg * Wg)), axis=2).reshape(N, C, Hg, Wg)
                return vals * valid[:, None, :, :]
            wx1 = (ix - ix0)[:, None]
            wy1 = (iy - iy0)[:, None]
            wx0 = 1.0 - wx1
            wy0 = 1.0 - wy1
            return gather(ix0, iy0) * wx0 * wy0 + gather(ix0 + 1.0, iy0) * wx1 * wy0 + gather(ix0, iy0 + 1.0) * wx0 * wy1 + gather(ix0 + 1.0, iy0 + 1.0) * wx1 * wy1

        def _forward(x, ln_w, ln_b, wq, wk, wv, w_out, b_out, off_dw_w, off_dw_b, off_pw_w, cpb_w1, cpb_b1, cpb_w2, cpb_b2, cpb_w3, cpb_b3):
            b, c, Hf, Wf = x.shape
            mu = x.mean(axis=1, keepdims=True)
            var = ((x - mu) ** 2).mean(axis=1, keepdims=True)
            xn = (x - mu) / jnp.sqrt(var + 1e-06) * ln_w[None, :, None, None] + ln_b[None, :, None, None]
            xp = xn.reshape(b, c, 4, 8, 4, 8).transpose(2, 4, 0, 1, 3, 5).reshape(16 * b, c, 8, 8)
            B, C, H, W = xp.shape
            xg = xp.reshape(B, G, OFF_DIMS, H, W)
            q = jnp.einsum('bgihw,goi->bgohw', xg, wq)
            gq = q.reshape(B * G, OFF_DIMS, H, W)
            t = jax.lax.conv_general_dilated(gq, off_dw_w, (DS, DS), [(1, 1), (1, 1)], dimension_numbers=('NCHW', 'OIHW', 'NCHW'), feature_group_count=OFF_DIMS)
            t = jax.nn.gelu(t + off_dw_b[None, :, None, None], approximate=False)
            off = jnp.tanh(jnp.einsum('bchw,oc->bohw', t, off_pw_w)) * OFF_SCALE
            Hp, Wp = off.shape[-2:]
            gx, gy = jnp.meshgrid(jnp.arange(Wp, dtype=x.dtype), jnp.arange(Hp, dtype=x.dtype), indexing='xy')
            vx = gx[None] + off[:, 0]
            vy = gy[None] + off[:, 1]
            vgrid = jnp.stack([2.0 * vx / max(Hp - 1, 1) - 1.0, 2.0 * vy / max(Wp - 1, 1) - 1.0], axis=-1)
            kv = _grid_sample(xp.reshape(B * G, OFF_DIMS, H, W), vgrid).reshape(B, G, OFF_DIMS, Hp, Wp)
            k = jnp.einsum('bgihw,goi->bgohw', kv, wk).reshape(B, HEADS, DIM_HEAD, Hp * Wp)
            v = jnp.einsum('bgihw,goi->bgohw', kv, wv).reshape(B, HEADS, DIM_HEAD, Hp * Wp)
            qh = (q * SCALE).reshape(B, HEADS, DIM_HEAD, H * W)
            sim = jnp.einsum('bhdi,bhdj->bhij', qh, k)
            gxq, gyq = jnp.meshgrid(jnp.arange(W, dtype=x.dtype), jnp.arange(H, dtype=x.dtype), indexing='xy')
            qgrid = jnp.stack([2.0 * gxq / max(H - 1, 1) - 1.0, 2.0 * gyq / max(W - 1, 1) - 1.0], axis=-1).reshape(H * W, 2)
            kvgrid = vgrid.reshape(B * G, Hp * Wp, 2)
            pos = qgrid[None, :, None, :] - kvgrid[:, None, :, :]
            bias = jnp.sign(pos) * jnp.log1p(jnp.abs(pos))
            bias = jax.nn.relu(bias @ cpb_w1.T + cpb_b1)
            bias = jax.nn.relu(bias @ cpb_w2.T + cpb_b2)
            bias = bias @ cpb_w3.T + cpb_b3
            sim = sim + bias.reshape(B, HEADS, H * W, Hp * Wp)
            attn = jax.nn.softmax(sim, axis=-1)
            out = jnp.einsum('bhij,bhdj->bhdi', attn, v).reshape(B, DIM, H, W)
            out = jnp.einsum('bchw,oc->bohw', out, w_out) + b_out[None, :, None, None]
            return out.reshape(4, 4, b, c, 8, 8).transpose(2, 3, 0, 4, 1, 5).reshape(b, c, Hf, Wf)
        return _forward(x, ln_w, ln_b, wq, wk, wv, w_out, b_out, off_dw_w, off_dw_b, off_pw_w, cpb_w1, cpb_b1, cpb_w2, cpb_b2, cpb_w3, cpb_b3)

    def _gn(v, G=32, eps=1e-5):
        B_, C_, H_, W_ = v.shape
        g = v.reshape(B_, G, C_ // G, H_, W_)
        m = jnp.mean(g, axis=(2, 3, 4), keepdims=True)
        s = jnp.var(g, axis=(2, 3, 4), keepdims=True)
        return ((g - m) / jnp.sqrt(s + eps)).reshape(v.shape)

    def _ln_c(v, eps=1e-6):
        m = jnp.mean(v, axis=1, keepdims=True)
        s = jnp.var(v, axis=1, keepdims=True)
        return (v - m) / jnp.sqrt(s + eps)

    def _ln_t(v, eps=1e-5):
        m = jnp.mean(v, axis=-1, keepdims=True)
        s = jnp.var(v, axis=-1, keepdims=True)
        return (v - m) / jnp.sqrt(s + eps)

    def _to_tokens(v):
        B_, C_, H_, W_ = v.shape
        return v.reshape(B_, C_, H_ * W_).transpose(0, 2, 1)
    def _from_tokens(t, like):
        B_, C_, H_, W_ = like.shape
        return t.transpose(0, 2, 1).reshape(B_, C_, H_, W_)

    x = x + _L0_conv_ref(_gn(x), L0_conv_Wqkv, L0_conv_bqkv, L0_conv_Wout, L0_conv_bout)
    x = x + _L1_conv_ref(_gn(x), L1_conv_ln_w, L1_conv_ln_b, L1_conv_wq, L1_conv_wk, L1_conv_wv, L1_conv_w_out, L1_conv_b_out, L1_conv_off_dw_w, L1_conv_off_dw_b, L1_conv_off_pw_w, L1_conv_cpb_w1, L1_conv_cpb_b1, L1_conv_cpb_w2, L1_conv_cpb_b2, L1_conv_cpb_w3, L1_conv_cpb_b3)
    return x


_drawn_inputs = setup_inputs


def setup_inputs(seed=0):
    import zlib

    import numpy as np

    out = dict(_drawn_inputs(seed))
    spreads = {'L1_conv_ln_w': (1.0, 0.545),
     'L1_conv_ln_b': (0.0, 1.329),
     'L1_conv_b_out': (0.0, 0.336),
     'L1_conv_off_dw_b': (0.0, 0.1),
     'L1_conv_cpb_b1': (0.0, 0.8),
     'L1_conv_cpb_b2': (0.0, 2.0)}
    factors = {'L0_conv_Wqkv': 4.73,
     'L0_conv_bqkv': 3.851,
     'L0_conv_Wout': 2.943,
     'L1_conv_wk': 23.252,
     'L1_conv_cpb_w1': 8.0,
     'L1_conv_cpb_w2': 8.0,
     'L1_conv_cpb_w3': 8.0,
     'L0_conv_bout': 8.0}
    for name, (base, spread) in spreads.items():
        noise = np.random.default_rng([zlib.crc32(name.encode()), seed]).standard_normal(out[name].shape)
        drawn = base * np.exp(spread * noise) if base else spread * noise
        out[name] = jnp.asarray(drawn.astype(out[name].dtype))
    for name, factor in factors.items():
        out[name] = (out[name] * factor).astype(out[name].dtype)
    return out
```

```python
from contextlib import ExitStack

import concourse.bass as bass
from concourse import mybir

ALU = mybir.AluOpType
ACT = mybir.ActivationFunctionType
F32 = mybir.dt.float32
F32R = mybir.dt.float32r
BF16 = mybir.dt.bfloat16
AX = mybir.AxisListType

P = 128
B, C, HW = 8, 512, 1024
CT = C // P
HEADS, D = 8, 64
PAIRS = HEADS // 2
KT = HW // P
TILES = HEADS * KT
GROUP_TILES = 8
WIN = 16
PX = 64
PTS = 4
PXT = HW // P
GN_EPS, LN_EPS = 1e-5, 1e-6
UNITS = WIN * PTS // 2
ROWS = 7
SEG = WIN * PTS * C // 4

QSTEP, KSTEP = 4, 5


def ring_uses():
    names = [("v", n) for n in range(4)] + [("q", 0), ("k", 0), ("s", 0), ("s", 1)]
    for m in range(TILES):
        if m + 2 < TILES:
            names.append(("s", m + 2))
        if m // 16 + 1 < PAIRS and m % 16 == QSTEP:
            names.append(("q", m // 16 + 1))
        if m // 16 + 1 < PAIRS and m % 16 == KSTEP:
            names.append(("k", m // 16 + 1))
    names += [("o0", n) for n in range(CT)]
    names += [("tp", n) for n in range(4)] + [("tc", n) for n in range(CT)] + [("lq", n) for n in range(CT)]
    names += [("kv", 0), ("kvp", 0), ("sim", 0)]
    names += [("h2", n) for n in range(UNITS)] + [("bt", 0)]
    names += [("at", n) for n in range(CT)] + [("av", n) for n in range(CT)] + [("o1", n) for n in range(CT)]
    return {name: n for n, name in enumerate(names)}


USE = ring_uses()
assert len(USE) % 2 == 0
RING_PER = len(USE) // 2

DVE_STEPS = 39


def build(nc, x, wqkv, bqk, bv, wo0, bo0, lnw, lnb, wqT, wkT, wvT, woT, bo1, dww, dwb, pwT,
          w1T, b1, w2T, b2, w3c, b3, c_ident, c_gavg, c_gxy, c_grid, out):
    with ExitStack() as ctx:
        def sb(name, shape, dt=F32):
            return ctx.enter_context(nc.sbuf_tensor(name, shape, dt))

        def sem(name):
            return ctx.enter_context(nc.semaphore(name))

        W = sb("w_qkv", [P, CT, 3 * C])
        WO0 = sb("w_out0", [P, CT, C])
        WO1 = sb("w_out1", [P, CT, C])
        WQB = sb("wq_blocks", [P, CT, P])
        WKB = sb("wk_blocks", [P, CT, P])
        WVB = sb("wv_blocks", [P, CT, P])
        BQK = sb("b_qk", [P, 8])
        VB = sb("b_v", [P, C])
        BO0 = sb("b_out0", [P, CT])
        BO1 = sb("b_out1", [P, CT])
        LNW = sb("ln_w", [P, C])
        LNB = sb("ln_b", [P, C])
        CW = sb("conv_w", [P, 36])
        CB = sb("conv_b", [P, 1])
        PWZ = sb("off_pw", [P, 4])
        WB1 = sb("mlp_w1b1", [3, P])
        WB1R = sb("mlp_w1_rest", [3, P])
        WB1P = sb("mlp_w1_parts", [3, 3, P], BF16)
        W1R = sb("mlp_w1_rows", [P, P], BF16)
        W2 = sb("mlp_w2", [P, P])
        W2H = sb("mlp_w2_hi", [P, P], F32R)
        W2L = sb("mlp_w2_lo", [P, P], F32R)
        B2 = sb("mlp_b2", [P, 1])
        W3Z = sb("mlp_w3_slide", [P, 63])
        B3 = sb("mlp_b3", [P, 1])
        IDENT = sb("ident", [P, P])
        GAVG = sb("group_average", [P, P])
        GXY = sb("point_grid", [64, 16])
        GRID = sb("pixel_grid", [64, 16])
        NEGHALF = sb("neg_half", [P, 8])
        ONES = sb("ones", [P, SEG * 4 // P], BF16)

        X = sb("x_image", [P, CT, HW])
        QK = sb("qk_stacks", [P, 2, 3, 2, HW], F32R)
        arena = sb("arena", [P, 19456])
        V = arena[:, 0:4096].rearrange("p (t c) -> p t c", c=C)
        PB = arena[:, 4096:7168].rearrange("p (n k) -> p n k", n=3)
        PT = arena[:, 7168:15360].rearrange("p (h t q) -> p h t q", h=2, t=KT)
        OT = arena[:, 15360:19456].rearrange("p (t q) -> p t q", t=CT)
        A = arena[:, 0:4096].rearrange("p (t q) -> p t q", t=CT)
        XP = arena[:, 4096:8192].rearrange("p (t c) -> p t c", t=PXT)
        OL = arena[:, 4096:8192].rearrange("p (t q) -> p t q", t=CT)
        Q1 = arena[:, 8192:12288].rearrange("p (t q) -> p t q", t=CT)
        AZ = arena[:, 8192:12288]
        RR = arena[:, 12288:16384].bitcast(BF16)
        PROD = arena[:, 12288:15488].rearrange("p (n e) -> p n e", n=2)
        YS = arena[:, 12288:14336].rearrange("p (n q) -> p n q", n=2)
        H2 = arena[:, 16384:19456].rearrange("p (n q) -> p n q", n=3)
        E = arena[0:64, 16384:17920].bitcast(BF16).rearrange("p (b c) -> p b c", b=6)
        LNI = arena[0:64, 18432:18688].rearrange("p (a b) -> p a b", a=2)
        LNO = arena[0:64, 18688:18944].rearrange("p (a b) -> p a b", a=2)
        HAT = arena[0:64, 18944:19072].rearrange("p (a b) -> p a b", b=8)
        BSR = arena[:, 16384:16896]
        BS = arena[:, 16896:17152].rearrange("p (b t e) -> p b t e", b=PXT, t=CT)
        XR = PB
        H1H = QK[:, 0, 0]
        H1L = QK[:, 0, 1]

        PAUSE = sb("pause_dve", [P, 1])
        POOL_PAUSE = sb("pause_pool", [P, 1])
        PW = sb("pixel_weights", [P, C])
        BNS = sb("bn_stats", [P, CT, 2, 6])
        GST = sb("channel_stats", [P, CT, 2])
        GSS = sb("group_stats", [P, CT, 2])
        SQ = sb("mean_squares", [P, CT])
        GVE = sb("group_var", [P, CT])
        GRS = sb("group_rstd", [P, CT])
        LVE = sb("ln_var", [P, PXT])
        LRS = sb("ln_rstd", [P, PXT])
        LNS = sb("ln_bn", [P, PXT, 6])
        LMV = sb("ln_mean_var", [P, PXT, 2])
        NM = sb("neg_max", [P, TILES])
        SS = sb("exp_sums", [P, TILES])
        RC = sb("recips", [P, GROUP_TILES])
        RT = sb("recips_T", [GROUP_TILES, P])
        RB = sb("recips_b", [P, 512])
        T4 = sb("conv_sums", [P, 256])
        TG = sb("conv_gelu", [P, CT, 64])
        OFF = sb("offsets", [64, 16])
        VXY = sb("vgrid", [64, 16])
        IXY = sb("sample_xy", [64, 16])
        WT = sb("pixel_weights_T", [P, PXT, CT, 16])
        KV = sb("sampled", [P, CT, 64])
        KZ = sb("k_blocks", [P, CT, WIN, 8])
        VZ = sb("v_blocks", [P, CT, P])
        FP = sb("log_parts", [64, 3, P], BF16)
        FR = sb("log_rest", [64, P])
        SM = sb("sim", [P, PXT * CT, 8])
        SMX = sb("sim_max", [P, 64])
        SMS = sb("sim_sum", [P, 64])

        BIG = ctx.enter_context(nc.psum_tensor("big", [P, 2, HW], F32))
        TB = ctx.enter_context(nc.psum_tensor("turned", [P, 2, 512], F32))
        OB = ctx.enter_context(nc.psum_tensor("out_acc", [P, 512], F32))
        MB = ctx.enter_context(nc.psum_tensor("misc", [P, 512], F32))

        rows_dram = nc.dram_tensor("mlp_rows", [ROWS, WIN * PTS * C], BF16).ap()
        w1_dram = nc.dram_tensor("mlp_w1_dram", [3, ROWS, P], BF16).ap()

        zeroed = sem("zeroed")
        w_in = sem("w_in")
        w1_out = sem("w1_out")
        w1_in = sem("w1_in")
        w1_split = sem("w1_split")
        w_ready = sem("w_ready")
        full = [sem("ring_full0"), sem("ring_full1")]
        free = [sem("ring_free0"), sem("ring_free1")]
        x_in = sem("x_in")
        gn_in = sem("gn_in")
        gn_sum = sem("gn_sum")
        gn_var = sem("gn_var")
        gn_rstd = sem("gn_rstd")
        xn = sem("xn")
        q_hi = sem("q_hi")
        k_hi = sem("k_hi")
        dup = sem("dup")
        mx = sem("mx")
        t_full = [sem("turned_full0"), sem("turned_full1")]
        t_free = [sem("turned_free0"), sem("turned_free1")]
        av_full = sem("av_full")
        ot_done = sem("ot_done")
        rc_done = sem("rc_done")
        rc_turned = sem("rc_turned")
        rt_done = sem("rt_done")
        rb_full = sem("rb_full")
        rb_done = sem("rb_done")
        xr_in = [sem("xr_in0"), sem("xr_in1")]
        gnorm = sem("gnorm")
        ln_var = sem("ln_var")
        ln_rstd = sem("ln_rstd")
        xp_done = sem("xp_done")
        conv_done = sem("conv_done")
        gelu_done = sem("gelu_done")
        off_full = sem("off_full")
        off_done = sem("off_done")
        pw_done = sem("pw_done")
        pw_turned = sem("pw_turned")
        wt_done = sem("wt_done")
        log_in = sem("log_in")
        log_out = sem("log_out")
        e_done = sem("e_done")
        rows_out = sem("rows_out")
        rows_in = sem("rows_in")
        az_zero = sem("az_zero")
        h1_full = sem("h1_full")
        h1_hi = sem("h1_hi")
        h1_done = sem("h1_done")
        l3_done = sem("l3_done")
        bsr_done = sem("bsr_done")
        sm_in = sem("sm_in")
        sm_exp = sem("sm_exp")
        az_done = sem("az_done")
        y_out = [sem("y_out0"), sem("y_out1")]
        dve_step = sem("dve_step")
        pool_step = sem("pool_step")

        def slot(name):
            return BIG[:, USE[name] % 2]

        def wait_full(eng, name, i):
            eng.wait_ge(full[USE[name] % 2], i * RING_PER + USE[name] // 2 + 1)

        def wait_free(eng, name, i):
            eng.wait_ge(free[USE[name] % 2], i * RING_PER + USE[name] // 2 + 1)

        def wait_emptied(eng, name, i):
            eng.wait_ge(free[USE[name] % 2], i * RING_PER + USE[name] // 2 + 2)

        def filled(ins, name):
            ins.then_inc(full[USE[name] % 2], 1)

        def freed(ins, name):
            ins.then_inc(free[USE[name] % 2], 1)

        def az_window(w):
            at = AZ[w * 64:(w + 1) * 64, w * 4:w * 4 + 1]
            return bass.AP(at.tensor, at.offset, [[at.ap[0][0], 64], [C + 8, PXT], [64, 8], [1, 4]])

        block = ctx.enter_context(nc.Block())

        @block.sync
        def _(sp):
            loads = [(W[:], wqkv.rearrange("(t p) n -> p t n", p=P)),
                     (WO0[:], wo0.rearrange("(t p) n -> p t n", p=P)),
                     (WO1[:], woT.rearrange("(t p) n -> p t n", p=P)),
                     (BQK[:], bqk), (BO0[:], bo0), (BO1[:], bo1),
                     (VB[:], bv.partition_broadcast(P)), (LNW[:], lnw.partition_broadcast(P)),
                     (LNB[:], lnb.partition_broadcast(P)), (W2[:], w2T), (B2[:], b2),
                     (B3[:], b3.partition_broadcast(P)), (WB1[0:2], w1T), (WB1[2:3], b1),
                     (IDENT[:], c_ident), (GAVG[:], c_gavg), (GXY[:], c_gxy), (GRID[:], c_grid)]
            for h in range(2):
                rows = slice(64 * h, 64 * h + 64)
                loads += [(CW[rows], dww), (CB[rows], dwb)]
            for dst, src in loads:
                sp.dma_start(dst, src).then_inc(w_in, 16)
            sp.wait_ge(zeroed, 1)
            padded = [(W3Z[:, 31:32], w3c)]
            for h in range(2):
                rows = slice(64 * h, 64 * h + 64)
                padded.append((PWZ[rows, 2 * h:2 * h + 2], pwT))
                for dst, src in ((WQB, wqT), (WKB, wkT), (WVB, wvT)):
                    padded.append((dst[rows, :, rows], src.rearrange("(t h) i o -> h i t o", h=2)[h]))
            for dst, src in padded:
                sp.dma_start(dst, src).then_inc(w_in, 16)
            assert len(loads) + len(padded) == N_LOADS
            sp.wait_ge(w1_split, 1)
            for j in range(3):
                sp.dma_start(w1_dram[:, 2 * j:2 * j + 2].rearrange("i c m -> c i m"),
                             WB1P[0:2]).then_inc(w1_out, 16)
            sp.dma_start(w1_dram[:, 6:7].rearrange("i c m -> c i m"), WB1P[2:3]).then_inc(w1_out, 16)
            sp.dma_start(rows_dram[6].rearrange("(p n) -> p n", p=P), ONES[:]).then_inc(w1_out, 16)
            sp.wait_ge(w1_out, 16 * 5)
            for s in range(4):
                sp.dma_start(W1R[32 * s:32 * s + 3 * ROWS], w1_dram.rearrange("i b m -> (i b) m")).then_inc(w1_in, 16)

            with sp.Fori(0, B) as i:
                xi = x[i].rearrange("(t p) n -> p t n", p=P)
                yi = out[i].rearrange("(t p) n -> p t n", p=P)
                assert USE[("o1", CT - 1)] == len(USE) - 1
                sp.wait_ge(free[1], i * RING_PER + 1)
                sp.dma_start(X[:], xi).then_inc(x_in, 16)
                for p in range(PAIRS):
                    wait_emptied(sp, ("k", p), i)
                    for part in (1, 2):
                        for h in range(2):
                            own, other = slice(64 * h, 64 * h + 64), slice(64 - 64 * h, 128 - 64 * h)
                            sp.dma_start(QK[other, p % 2, part, h].bitcast(F32),
                                         QK[own, p % 2, part, h].bitcast(F32)).then_inc(dup, 16)
                sp.wait_ge(t_full[1], i * TILES + TILES + 3)
                for t in range(CT):
                    if t >= 2:
                        wait_emptied(sp, ("o0", t - 2), i)
                    sp.dma_start(XR[:, t % 2], xi[:, t]).then_inc(xr_in[t % 2], 16)
                sp.wait_ge(e_done, i + 1)
                sp.dma_start(rows_dram[0:6].rearrange("b (p n) -> p b n", p=64), E).then_inc(rows_out, 16)
                sp.wait_ge(rows_out, i * 16 + 16)
                for s in range(4):
                    for d in range(3):
                        sp.dma_start(RR[32 * s + ROWS * d:32 * s + ROWS * d + ROWS],
                                     rows_dram[:, SEG * s:SEG * (s + 1)]).then_inc(rows_in, 16)
                for t in range(CT):
                    wait_emptied(sp, ("o1", t), i)
                    sp.dma_start(yi[:, t], YS[:, t % 2]).then_inc(y_out[t % 2], 16)
            for s in range(2):
                sp.wait_ge(y_out[s], 16 * B * CT // 2 + 16)

        @block.gpsimd
        def _(pool):
            pool.memset(NEGHALF[:], -0.5).then_inc(pool_step, 1)
            pool.wait_ge(pool_step, 1)
            with pool.Fori(0, B) as i:
                def rstd(dst, src, n, ready, done, k):
                    pool.wait_ge(ready, k)
                    pool.tensor_tensor(dst, src, NEGHALF[:, 0:n], ALU.pow).then_inc(done, 1)

                rstd(GRS[:], GVE[:], CT, gn_var, gn_rstd, i * 2 + 1)
                rstd(GRS[:], GVE[:], CT, gn_var, gn_rstd, i * 2 + 2)
                rstd(LRS[:], LVE[:], PXT, ln_var, ln_rstd, i + 1)
                wait_emptied(pool, ("sim", 0), i)
                pool.tensor_tensor(POOL_PAUSE[:], NEGHALF[:, 0:1], NEGHALF[:, 0:1], ALU.mult)
                pool.memset(AZ, 0.0).then_inc(az_zero, 1)

        @block.tensor
        def _(pe):
            def project(name, i, weights, n0, moving):
                wait_free(pe, name, i)
                for n in range(2):
                    for k in range(CT):
                        mm = pe.matmul(slot(name)[:, 512 * n:512 * n + 512], weights[:, k, n0:n0 + P],
                                       moving[:, k, 512 * n:512 * n + 512], start=(k == 0), stop=(k == CT - 1))
                filled(mm, name)

            def scores(m, i):
                p, hf, h, j = m // 16, m // 8 % 2, m // 4 % 2, m % 4
                wait_free(pe, ("s", m), i)
                if m % 16 == 0:
                    pe.wait_ge(dup, (i * PAIRS + p + 1) * 64)
                q0 = 512 * hf + 128 * j
                for n in range(2):
                    for part in (1, 2):
                        mm = pe.matmul(slot(("s", m))[:, 512 * n:512 * n + 512], QK[:, p % 2, 0, h, q0:q0 + P],
                                       QK[:, p % 2, part, h, 512 * n:512 * n + 512],
                                       start=(part == 1), stop=(part == 2))
                filled(mm, ("s", m))

            def turn(m, i):
                wait_emptied(pe, ("s", m), i)
                for half in range(2):
                    pe.wait_ge(t_free[half], i * TILES + m + 1)
                    for k in range(4):
                        kt = 4 * half + k
                        mm = pe.transpose(TB[:, half, k * P:(k + 1) * P], PB[:, m % 3, kt * P:(kt + 1) * P], IDENT[:])
                    mm.then_inc(t_full[half], 1)

            def value_product(g, i):
                p = g // 2
                pe.wait_ge(t_free[0], i * TILES + 8 * g + 9)
                pe.wait_ge(t_free[1], i * TILES + 8 * g + 9)
                pe.wait_ge(ot_done, i * 8 + g + 1)
                for kt in range(KT):
                    for h in range(2):
                        hc = (2 * p + h) * D
                        mm = pe.matmul(OB[D * h:D * h + D, :], V[:, kt, hc:hc + D], PT[:, h, kt],
                                       start=(kt == 0), stop=(kt == KT - 1))
                mm.then_inc(av_full, 1)
                pe.wait_ge(rc_done, i * 8 + g + 1)
                pe.transpose(MB[0:8, 0:P], RC[:], IDENT[:]).then_inc(rc_turned, 1)

            def spread_recips(g, i):
                pe.wait_ge(rt_done, i * 8 + g + 1)
                for j in range(4):
                    for h in range(2):
                        row = 4 * h + j
                        mm = pe.matmul(MB[D * h:D * h + D, P * j:P * (j + 1)],
                                       IDENT[0:8, row:row + 1].broadcast_to([8, D]), RT[:],
                                       start=(j == 0), stop=True, skip_group_check=True)
                mm.then_inc(rb_full, 1)

            pe.wait_ge(w_in, 16 * N_LOADS)
            pe.wait_ge(w_ready, 1)
            pe.wait_ge(w1_in, 64)
            with pe.Fori(0, B) as i:
                pe.wait_ge(gn_in, i * 2 + 1)
                pe.matmul(MB[:, 0:8], GAVG[:], GST[:].rearrange("p t s -> p (t s)"), start=True, stop=True)\
                    .then_inc(gn_sum, 1)
                pe.wait_ge(xn, i * CT + CT)
                for n in range(4):
                    wait_free(pe, ("v", n), i)
                    for s in range(2):
                        tt = 2 * n + s
                        for k in range(CT):
                            mm = pe.matmul(slot(("v", n))[:, 512 * s:512 * s + 512], X[:, k, P * tt:P * tt + P],
                                           W[:, k, 2 * C:3 * C], start=(k == 0), stop=(k == CT - 1))
                    filled(mm, ("v", n))
                project(("q", 0), i, W, 0, X)
                project(("k", 0), i, W, C, X)
                scores(0, i)
                scores(1, i)
                for m in range(TILES):
                    turn(m, i)
                    if m + 2 < TILES:
                        scores(m + 2, i)
                    nxt = m // 16 + 1
                    if nxt < PAIRS and m % 16 == QSTEP:
                        project(("q", nxt), i, W, P * nxt, X)
                    if nxt < PAIRS and m % 16 == KSTEP:
                        project(("k", nxt), i, W, C + P * nxt, X)
                    if m % 8 == 0 and m:
                        value_product(m // 8 - 1, i)
                    if m % 8 == 1 and m > 1:
                        spread_recips(m // 8 - 1, i)
                value_product(7, i)
                spread_recips(7, i)
                pe.wait_ge(ot_done, i * 8 + 9)
                for t in range(CT):
                    project(("o0", t), i, WO0, P * t, OT)

                pe.wait_ge(gn_in, i * 2 + 2)
                pe.matmul(MB[:, 0:8], GAVG[:], GST[:].rearrange("p t s -> p (t s)"), start=True, stop=True)\
                    .then_inc(gn_sum, 1)
                pe.wait_ge(gnorm, i * CT + CT)
                for n in range(4):
                    wait_free(pe, ("tp", n), i)
                    for s in range(2):
                        for t in range(CT):
                            mm = pe.transpose(slot(("tp", n))[:, 512 * s + P * t:512 * s + P * (t + 1)],
                                              A[:, t, P * (2 * n + s):P * (2 * n + s + 1)], IDENT[:])
                    filled(mm, ("tp", n))
                pe.wait_ge(xp_done, i + 1)
                for t in range(CT):
                    wait_free(pe, ("tc", t), i)
                    for r in range(PXT):
                        mm = pe.transpose(slot(("tc", t))[:, P * r:P * (r + 1)], XP[:, r, P * t:P * (t + 1)], IDENT[:])
                    filled(mm, ("tc", t))
                for t in range(CT):
                    wait_free(pe, ("lq", t), i)
                    wait_emptied(pe, ("tc", t), i)
                    for n in range(2):
                        mm = pe.matmul(slot(("lq", t))[:, 512 * n:512 * n + 512], WQB[:, t],
                                       A[:, t, 512 * n:512 * n + 512], start=True, stop=True)
                    filled(mm, ("lq", t))
                pe.wait_ge(gelu_done, i + 1)
                for t in range(CT):
                    mm = pe.matmul(MB[0:64, 4 * t:4 * t + 4], TG[:, t], PWZ[:], start=(t == 0), stop=True,
                                   skip_group_check=True)
                mm.then_inc(off_full, 1)
                pe.wait_ge(pw_done, i + 1)
                for t in range(CT):
                    mm = pe.transpose(MB[:, P * t:P * t + P], PW[:, P * t:P * t + P], IDENT[:])
                mm.then_inc(pw_turned, 1)
                pe.wait_ge(wt_done, i + 1)
                wait_free(pe, ("kv", 0), i)
                for r in range(PXT):
                    for t in range(CT):
                        c0 = (r * CT + t) * 16
                        mm = pe.matmul(slot(("kv", 0))[:, c0:c0 + 16], XP[:, r, P * t:P * t + P], WT[:, r, t],
                                       start=(c0 == 0), stop=True, skip_group_check=True)
                filled(mm, ("kv", 0))
                wait_emptied(pe, ("kv", 0), i)
                wait_free(pe, ("kvp", 0), i)
                for t in range(CT):
                    pe.matmul(slot(("kvp", 0))[:, 64 * t:64 * t + 64], WKB[:, t], KV[:, t],
                              start=(t == 0), stop=True, skip_group_check=True)
                    mm = pe.matmul(slot(("kvp", 0))[0:64, 512 + P * t:512 + P * t + P], KV[:, t], WVB[:, t],
                                   start=(t == 0), stop=True, skip_group_check=True)
                filled(mm, ("kvp", 0))
                wait_emptied(pe, ("kvp", 0), i)
                wait_free(pe, ("sim", 0), i)
                for r in range(PXT):
                    for t in range(CT):
                        c0 = (r * CT + t) * 16
                        mm = pe.matmul(slot(("sim", 0))[:, c0:c0 + 16], Q1[:, t, P * r:P * r + P],
                                       KZ[:, t, 2 * r:2 * r + 2].rearrange("p u e -> p (u e)"),
                                       start=(c0 == 0), stop=True, skip_group_check=True)
                filled(mm, ("sim", 0))

                def mlp1(u):
                    if u:
                        pe.wait_ge(h1_done, i * UNITS + u)
                    for w in range(2):
                        row = 2 * u + w
                        s, o = row // 16, row % 16 * 512
                        rows = slice(32 * s, 32 * s + 3 * ROWS)
                        mm = pe.matmul(TB[:, w], W1R[rows], RR[rows, o:o + 512], start=True, stop=True)
                    mm.then_inc(h1_full, 1)

                def mlp2(u):
                    wait_free(pe, ("h2", u), i)
                    pe.wait_ge(h1_done, i * UNITS + u + 1)
                    ops = ((W2H, H1H), (W2H, H1L), (W2L, H1H))
                    for n, (w, h) in enumerate(ops):
                        for c in range(2):
                            mm = pe.matmul(slot(("h2", u))[:, 512 * c:512 * c + 512], w[:],
                                           h[:, u % 2, 512 * c:512 * c + 512], start=(n == 0), stop=(n == 2))
                    filled(mm, ("h2", u))

                def mlp3(v):
                    wait_emptied(pe, ("h2", 2 * v), i)
                    wait_emptied(pe, ("h2", 2 * v + 1), i)
                    for j in range(4):
                        mm = pe.matmul(OB[32 * j:32 * j + 32, :], W3Z[:, 31 - v:63 - v],
                                       H2[:, (2 * v + j // 2) % 3, 512 * (j % 2):512 * (j % 2) + 512],
                                       start=(v == 0), stop=(v == WIN - 1), skip_group_check=True)
                    mm.then_inc(l3_done, 1)

                pe.wait_ge(rows_in, (i + 1) * 16 * 12)
                mlp1(0)
                for u in range(UNITS):
                    if u + 1 < UNITS:
                        mlp1(u + 1)
                    mlp2(u)
                    if u >= 2 and u % 2 == 0:
                        mlp3(u // 2 - 1)
                mlp3(WIN - 1)
                pe.wait_ge(bsr_done, i + 1)
                wait_free(pe, ("bt", 0), i)
                for t in range(CT):
                    mm = pe.transpose(slot(("bt", 0))[:, P * t:P * t + P], BSR[:, P * t:P * t + P], IDENT[:])
                filled(mm, ("bt", 0))
                pe.wait_ge(az_done, i * 2 + 2)
                for t in range(CT):
                    wait_free(pe, ("at", t), i)
                    for r in range(PXT):
                        c0 = (r * CT + t) * P
                        mm = pe.transpose(slot(("at", t))[:, P * r:P * r + P], AZ[:, c0:c0 + P], IDENT[:])
                    filled(mm, ("at", t))
                for t in range(CT):
                    wait_emptied(pe, ("at", t), i)
                    wait_free(pe, ("av", t), i)
                    for n in range(2):
                        mm = pe.matmul(slot(("av", t))[:, 512 * n:512 * n + 512], VZ[:, t],
                                       A[:, t, 512 * n:512 * n + 512], start=True, stop=True)
                    filled(mm, ("av", t))
                for t in range(CT):
                    wait_emptied(pe, ("av", t), i)
                for t in range(CT):
                    project(("o1", t), i, WO1, P * t, OL)

        @block.scalar
        def _(act):
            with act.Fori(0, B) as i:
                def high(name, part, first, p, done):
                    wait_full(act, (name, p), i)
                    for h in range(2):
                        rows = slice(64 * h, 64 * h + 64)
                        a = act.activation(QK[rows, p % 2, part, h], slot((name, p))[rows], ACT.Identity,
                                           bias=BQK[rows, first + p:first + p + 1])
                    a.then_inc(done, 1)

                def exp(m):
                    act.wait_ge(mx, i * TILES + m + 1)
                    act.wait_ge(t_full[1], i * TILES + m + 1)
                    freed(act.activation(PB[:, m % 3], slot(("s", m)), ACT.Exp, bias=NM[:, m:m + 1],
                                         accum_out=SS[:, m:m + 1]), ("s", m))

                def copy_turned(m):
                    act.wait_ge(t_full[0], i * TILES + m + 1)
                    if m % 8 == 0 and m:
                        act.wait_ge(av_full, i * 8 + m // 8)
                    h, j = m // 4 % 2, m % 4
                    act.activation(PT[:, h, 0:4, P * j:P * j + P], TB[:, 0].rearrange("p (k q) -> p k q", k=4),
                                   ACT.Copy).then_inc(t_free[0], 1)

                def copy_recips(g):
                    act.wait_ge(rc_turned, i * 8 + g + 1)
                    act.activation(RT[:], MB[0:8, 0:P], ACT.Copy).then_inc(rt_done, 1)

                def copy_spread(g):
                    act.wait_ge(rb_full, i * 8 + g + 1)
                    act.activation(RB[:], MB[:], ACT.Copy).then_inc(rb_done, 1)

                high("q", 0, 0, 0, q_hi)
                high("k", 1, 4, 0, k_hi)
                for m in range(-1, TILES):
                    if m + 1 < TILES:
                        exp(m + 1)
                    if m >= 0:
                        copy_turned(m)
                        nxt = m // 16 + 1
                        if nxt < PAIRS and m % 16 == QSTEP:
                            high("q", 0, 0, nxt, q_hi)
                        if nxt < PAIRS and m % 16 == KSTEP:
                            high("k", 1, 4, nxt, k_hi)
                        if m % 8 == 0 and m:
                            copy_recips(m // 8 - 1)
                        if m % 8 == 1 and m > 1:
                            copy_spread(m // 8 - 1)
                copy_recips(7)
                copy_spread(7)

                for n in range(4):
                    wait_full(act, ("tp", n), i)
                    freed(act.activation(XP[:, 2 * n:2 * n + 2].rearrange("p b c -> p (b c)"), slot(("tp", n)),
                                         ACT.Copy), ("tp", n))
                for t in range(CT):
                    wait_full(act, ("tc", t), i)
                    freed(act.activation(A[:, t], slot(("tc", t)), ACT.Copy), ("tc", t))
                for t in range(CT):
                    wait_full(act, ("lq", t), i)
                    freed(act.activation(Q1[:, t], slot(("lq", t)), ACT.Copy), ("lq", t))
                act.wait_ge(conv_done, i + 1)
                act.activation(TG[:].rearrange("p t c -> p (t c)"), T4[:], ACT.Gelu, bias=CB[:, 0:1])\
                    .then_inc(gelu_done, 1)
                act.wait_ge(off_full, i + 1)
                act.activation(OFF[:], MB[0:64, 0:16], ACT.Tanh).then_inc(off_done, 1)
                act.wait_ge(log_in, i + 1)
                act.activation(LNO.rearrange("p a b -> p (a b)"), LNI.rearrange("p a b -> p (a b)"),
                               ACT.Ln, bias=1.0).then_inc(log_out, 1)

                def relu1(u):
                    act.wait_ge(h1_full, i * UNITS + u + 1)
                    if u >= 2:
                        wait_full(act, ("h2", u - 2), i)
                    act.activation(H1H[:, u % 2], TB[:].rearrange("p s n -> p (s n)"), ACT.Relu).then_inc(h1_hi, 1)

                relu1(0)
                for u in range(UNITS):
                    if u + 1 < UNITS:
                        relu1(u + 1)
                    if u % 2 == 0:
                        wait_full(act, ("h2", u), i)
                        if u >= 3:
                            act.wait_ge(l3_done, i * WIN + (u - 3) // 2 + 1)
                        freed(act.activation(H2[:, u % 3], slot(("h2", u)), ACT.Relu, bias=B2[:, 0:1]), ("h2", u))
                act.wait_ge(l3_done, i * WIN + WIN)
                act.activation(BSR, OB[:], ACT.Identity, bias=B3[:, 0:1]).then_inc(bsr_done, 1)
                act.wait_ge(sm_in, i + 1)
                act.activation(SM[:].rearrange("p a b -> p (a b)"), SM[:].rearrange("p a b -> p (a b)"),
                               ACT.Exp).then_inc(sm_exp, 1)
                for t in (0, 2):
                    wait_full(act, ("at", t), i)
                    for a in range(4):
                        ins = act.activation(raster(A[:, t])[:, a], windowed(slot(("at", t)))[:, a], ACT.Copy)
                    freed(ins, ("at", t))
                for t in (0, 2):
                    wait_full(act, ("av", t), i)
                    freed(act.activation(OL[:, t], slot(("av", t)), ACT.Copy), ("av", t))

        @block.vector
        def _(dve):
            for t in (WQB, WKB, WVB, PWZ, W3Z, WT, KZ, VZ, PW):
                dve.memset(t[:], 0.0)
            dve.memset(ONES[:], 1.0).then_inc(zeroed, 1)
            for s in (free[0], free[1], t_free[0], t_free[1], ot_done):
                dve.sem_inc(s, 1)
            dve.sem_inc(t_full[1], 3)
            for s in (y_out[0], y_out[1]):
                dve.sem_inc(s, 16)
            dve.wait_ge(w_in, 16 * N_LOADS)
            steps = [0]

            def setup(ins):
                steps[0] += 1
                ins.then_inc(dve_step, 1)
                dve.wait_ge(dve_step, steps[0])

            dve.tensor_scalar(W[:, :, 0:C], W[:, :, 0:C], D ** -0.5, None, ALU.mult)
            dve.tensor_scalar(BQK[:, 0:4], BQK[:, 0:4], D ** -0.5, None, ALU.mult)
            setup(dve.tensor_copy(WB1P[:, 0], WB1[:]))
            setup(dve.tensor_tensor(WB1R[:], WB1[:], WB1P[:, 0], ALU.subtract))
            setup(dve.tensor_copy(WB1P[:, 1], WB1R[:]))
            setup(dve.tensor_tensor(WB1[:], WB1R[:], WB1P[:, 1], ALU.subtract))
            dve.tensor_copy(WB1P[:, 2], WB1[:]).then_inc(w1_split, 1)
            setup(dve.tensor_copy(W2H[:], W2[:]))
            dve.tensor_tensor(W2L[:], W2[:], W2H[:].bitcast(F32), ALU.subtract).then_inc(w_ready, 1)
            first = steps[0]

            with dve.Fori(0, B) as i:
                n_steps = [0]

                def link(ins):
                    n_steps[0] += 1
                    ins.then_inc(dve_step, 1)
                    dve.wait_ge(dve_step, i * DVE_STEPS + first + n_steps[0])

                def group_stats(k):
                    for t in range(CT):
                        for s in range(2):
                            ins = dve.bn_stats(BNS[:, t, s], X[:, t, 512 * s:512 * s + 512])
                    link(ins)
                    dve.memset(PAUSE[:], 0.0)
                    for t in range(CT):
                        ins = dve.bn_aggr(GST[:, t], BNS[:, t].rearrange("p s e -> p (s e)"))
                    link(ins)
                    link(dve.tensor_tensor(SQ[:], GST[:, :, 0], GST[:, :, 0], ALU.mult))
                    dve.tensor_tensor(GST[:, :, 1], GST[:, :, 1], SQ[:], ALU.add).then_inc(gn_in, 1)
                    dve.wait_ge(gn_sum, i * 2 + k + 1)
                    link(dve.tensor_copy(GSS[:].rearrange("p t s -> p (t s)"), MB[:, 0:8]))
                    link(dve.tensor_tensor(SQ[:], GSS[:, :, 0], GSS[:, :, 0], ALU.mult))
                    link(dve.tensor_tensor(GVE[:], GSS[:, :, 1], SQ[:], ALU.subtract))
                    dve.tensor_scalar(GVE[:], GVE[:], 0.0, GN_EPS, ALU.max, ALU.add).then_inc(gn_var, 1)
                    dve.wait_ge(gn_rstd, i * 2 + k + 1)

                def low(name, part, first_b, p, hi):
                    dve.wait_ge(hi, i * PAIRS + p + 1)
                    wait_full(dve, (name, p), i)
                    for h in range(2):
                        own, other = slice(64 * h, 64 * h + 64), slice(64 - 64 * h, 128 - 64 * h)
                        dst = QK[other, p % 2, 0, h] if name == "q" else QK[own, p % 2, 2, h]
                        ins = dve.scalar_tensor_tensor(out=dst, in0=slot((name, p))[own],
                                                       scalar=BQK[own, first_b + p:first_b + p + 1],
                                                       in1=QK[own, p % 2, part, h].bitcast(F32),
                                                       op0=ALU.add, op1=ALU.subtract)
                    freed(ins, (name, p))

                def row_max(m):
                    wait_full(dve, ("s", m), i)
                    dve.tensor_reduce(NM[:, m:m + 1], slot(("s", m)), AX.X, ALU.max, negate=True).then_inc(mx, 1)

                def copy_turned(m):
                    dve.wait_ge(t_full[1], i * TILES + m + 4)
                    if m % 8 == 0 and m:
                        dve.wait_ge(av_full, i * 8 + m // 8)
                    h, j = m // 4 % 2, m % 4
                    dve.tensor_copy(PT[:, h, 4:8, P * j:P * j + P], TB[:, 1].rearrange("p (k q) -> p k q", k=4))\
                        .then_inc(t_free[1], 1)

                def recips(g):
                    for m in (8 * g + 6, 8 * g + 7):
                        wait_emptied(dve, ("s", m), i)
                    dve.reciprocal(RC[:], SS[:, 8 * g:8 * g + 8]).then_inc(rc_done, 1)

                def outputs(g):
                    dve.wait_ge(rb_done, i * 8 + g + 1)
                    dve.wait_ge(av_full, i * 8 + g + 1)
                    dve.tensor_tensor(OT[:, g // 2, 512 * (g % 2):512 * (g % 2) + 512], OB[:], RB[:], ALU.mult)\
                        .then_inc(ot_done, 1)

                dve.wait_ge(x_in, i * 16 + 16)
                group_stats(0)
                for t in range(CT):
                    dve.tensor_scalar(X[:, t], X[:, t], GSS[:, t, 0:1], GRS[:, t:t + 1], ALU.subtract, ALU.mult)\
                        .then_inc(xn, 1)
                for n in range(4):
                    wait_full(dve, ("v", n), i)
                    freed(dve.tensor_tensor(V[:, 2 * n:2 * n + 2], slot(("v", n)).rearrange("p (s c) -> p s c", s=2),
                                            VB[:].unsqueeze(1).broadcast_to([P, 2, C]), ALU.add), ("v", n))
                low("q", 0, 0, 0, q_hi)
                low("k", 1, 4, 0, k_hi)
                for m in range(-1, TILES):
                    if m + 1 < TILES:
                        row_max(m + 1)
                    if m >= 0:
                        if m % 8 == 0 and m:
                            recips(m // 8 - 1)
                        copy_turned(m)
                        nxt = m // 16 + 1
                        if nxt < PAIRS and m % 16 == QSTEP + 1:
                            low("q", 0, 0, nxt, q_hi)
                        if nxt < PAIRS and m % 16 == KSTEP + 1:
                            low("k", 1, 4, nxt, k_hi)
                        if m % 8 == 2 and m > 2:
                            outputs(m // 8 - 1)
                recips(7)
                outputs(7)
                for t in range(CT):
                    wait_full(dve, ("o0", t), i)
                    dve.wait_ge(xr_in[t % 2], i * 32 + 16 * (t // 2) + 16)
                    freed(dve.scalar_tensor_tensor(out=X[:, t], in0=slot(("o0", t)), scalar=BO0[:, t:t + 1],
                                                   in1=XR[:, t % 2], op0=ALU.add, op1=ALU.add), ("o0", t))
                for t in (CT - 2, CT - 1):
                    wait_emptied(dve, ("o0", t), i)

                group_stats(1)
                for t in range(CT):
                    for a in range(4):
                        ins = dve.tensor_scalar(windowed(A[:, t])[:, a], raster(X[:, t])[:, a], GSS[:, t, 0:1],
                                                GRS[:, t:t + 1], ALU.subtract, ALU.mult)
                    ins.then_inc(gnorm, 1)
                for r in range(PXT):
                    if r % 2 == 0:
                        wait_emptied(dve, ("tp", r // 2), i)
                    ins = dve.bn_stats(LNS[:, r], XP[:, r])
                link(ins)
                dve.memset(PAUSE[:], 0.0)
                for r in range(PXT):
                    ins = dve.bn_aggr(LMV[:, r], LNS[:, r])
                link(ins)
                dve.tensor_scalar(LVE[:], LMV[:, :, 1], LN_EPS, None, ALU.add).then_inc(ln_var, 1)
                dve.wait_ge(ln_rstd, i + 1)
                for r in range(PXT):
                    ins = dve.scalar_tensor_tensor(out=XP[:, r], in0=XP[:, r], scalar=LMV[:, r, 0:1], in1=LNW[:],
                                                   op0=ALU.subtract, op1=ALU.mult)
                link(ins)
                for r in range(PXT):
                    ins = dve.scalar_tensor_tensor(out=XP[:, r], in0=XP[:, r], scalar=LRS[:, r:r + 1], in1=LNB[:],
                                                   op0=ALU.mult, op1=ALU.add)
                ins.then_inc(xp_done, 1)

                for t in range(CT):
                    wait_emptied(dve, ("lq", t), i)
                for s in range(2):
                    dve.wait_ge(y_out[s], i * 32 + 16)
                for n in range(4):
                    oy, ox = n // 2, n % 2
                    q = Q1.rearrange("p t (u y x) -> p (t u) y x", y=8, x=8)[:, :, 3 * oy:3 * oy + 5, 3 * ox:3 * ox + 5]
                    w = CW[:].rearrange("p (y x) -> p y x", y=6)[:, 1 - oy:6 - oy, 1 - ox:6 - ox]
                    prod = PROD[:, n % 2].rearrange("p (u y x) -> p u y x", y=5, x=5)
                    link(dve.tensor_tensor(prod, q, w.unsqueeze(1).broadcast_to([P, 64, 5, 5]), ALU.mult))
                    ins = dve.tensor_reduce(T4[:].rearrange("p (u o) -> p u o", o=4)[:, :, n],
                                            PROD[:, n % 2].rearrange("p (u e) -> p u e", e=25), AX.X, ALU.add)
                ins.then_inc(conv_done, 1)

                dve.wait_ge(off_done, i + 1)
                link(dve.scalar_tensor_tensor(out=VXY[:], in0=OFF[:], scalar=4.0, in1=GXY[:], op0=ALU.mult, op1=ALU.add))
                link(dve.tensor_scalar(VXY[:], VXY[:], 2.0, 1.0, ALU.mult, ALU.subtract))
                link(dve.tensor_scalar(IXY[:], VXY[:], 1.0, 8.0, ALU.add, ALU.mult))
                link(dve.tensor_scalar(IXY[:], IXY[:], 1.0, 0.5, ALU.subtract, ALU.mult))
                grid = GRID[:].rearrange("p (a b) -> p a b", a=2)
                pos = LNI[:, 0].rearrange("p (a b) -> p a b", b=8)
                link(dve.tensor_tensor(pos, grid[:, 1:2].broadcast_to([64, 16, 8]),
                                       VXY[:].unsqueeze(2).broadcast_to([64, 16, 8]), ALU.subtract))
                link(dve.tensor_scalar(LNI[:, 1], LNI[:, 0], -1.0, 0.0, ALU.mult, ALU.max))
                dve.tensor_scalar(LNI[:, 0], LNI[:, 0], 0.0, None, ALU.max).then_inc(log_in, 1)
                link(dve.tensor_tensor(HAT, grid[:, 0:1].broadcast_to([64, 16, 8]),
                                       IXY[:].unsqueeze(2).broadcast_to([64, 16, 8]), ALU.subtract))
                link(dve.scalar_tensor_tensor(out=HAT, in0=HAT, scalar=-1.0, in1=HAT, op0=ALU.mult, op1=ALU.max))
                link(dve.tensor_scalar(HAT, HAT, -1.0, 1.0, ALU.mult, ALU.add))
                link(dve.tensor_scalar(HAT, HAT, 0.0, None, ALU.max))
                hat = HAT.rearrange("p (g o) e -> p g o e", o=2)
                dve.tensor_tensor(PW[0:64].rearrange("p (g y x) -> p g y x", y=8, x=8),
                                  hat[:, :, 1].unsqueeze(3).broadcast_to([64, 8, 8, 8]),
                                  hat[:, :, 0].unsqueeze(2).broadcast_to([64, 8, 8, 8]), ALU.mult).then_inc(pw_done, 1)
                dve.wait_ge(log_out, i + 1)
                link(dve.tensor_tensor(FR[:], LNO[:, 0], LNO[:, 1], ALU.subtract))
                link(dve.tensor_copy(FP[:, 0], FR[:]))
                link(dve.tensor_tensor(FR[:], FR[:], FP[:, 0], ALU.subtract))
                link(dve.tensor_copy(FP[:, 1], FR[:]))
                link(dve.tensor_tensor(FR[:], FR[:], FP[:, 1], ALU.subtract))
                link(dve.tensor_copy(FP[:, 2], FR[:]))
                for part in range(3):
                    f = FP[:, part].rearrange("p (g o e) -> p g o e", o=2, e=8)
                    for o in range(2):
                        src = f[:, :, o].unsqueeze(2 if o == 0 else 3).broadcast_to([64, 8, 8, 8])
                        ins = dve.tensor_copy(E[:, 2 * part + o].rearrange("p (g y x) -> p g y x", y=8, x=8), src)
                ins.then_inc(e_done, 1)
                dve.wait_ge(pw_turned, i + 1)
                for g in range(2):
                    src = MB[64 * g:64 * g + 64].rearrange("p (t z b u e) -> p z b t u e", t=CT, z=2, b=PXT, u=2)[:, 0]
                    for w in range(2):
                        c0 = 8 * w + 4 * g
                        ins = dve.tensor_copy(WT[64 * w:64 * w + 64, :, :, c0:c0 + 4], src[:, :, :, w])
                ins.then_inc(wt_done, 1)
                wait_full(dve, ("kv", 0), i)
                for g in range(2):
                    src = slot(("kv", 0))[64 * g:64 * g + 64, 0:512].rearrange("p (b t u h e) -> p t b u h e",
                                                                               b=PXT, t=CT, u=2, h=2)
                    dst = KV[64 * g:64 * g + 64].rearrange("p t (b u e) -> p t b u e", b=PXT, u=2)
                    for w in range(2):
                        ins = dve.tensor_copy(dst[:, :, :, w], src[:, :, :, w, g])
                freed(ins, ("kv", 0))
                wait_full(dve, ("kvp", 0), i)
                for g in range(2):
                    rows = slice(64 * g, 64 * g + 64)
                    dve.tensor_scalar(KZ[rows, :, :, 4 * g:4 * g + 4],
                                      slot(("kvp", 0))[rows, 0:256].rearrange("p (t u e) -> p t u e", t=CT, u=WIN),
                                      D ** -0.5, None, ALU.mult)
                    ins = dve.tensor_copy(VZ[rows, :, rows],
                                          slot(("kvp", 0))[0:64, 512:1024].rearrange("p (t c) -> p t c", t=CT)[:, :, rows])
                freed(ins, ("kvp", 0))
                wait_full(dve, ("sim", 0), i)
                for w in range(2):
                    rows = slice(64 * w, 64 * w + 64)
                    ins = dve.tensor_copy(SM[rows], slot(("sim", 0))[rows, 0:512]
                                          .rearrange("p (n u e) -> p n u e", u=2, e=8)[:, :, w])
                freed(ins, ("sim", 0))

                def low1(u):
                    dve.wait_ge(h1_hi, i * UNITS + u + 1)
                    dve.scalar_tensor_tensor(out=H1L[:, u % 2], in0=TB[:].rearrange("p s n -> p (s n)"), scalar=0.0,
                                             in1=H1H[:, u % 2].bitcast(F32), op0=ALU.max, op1=ALU.subtract)\
                        .then_inc(h1_done, 1)

                low1(0)
                for u in range(UNITS):
                    if u + 1 < UNITS:
                        low1(u + 1)
                    if u % 2:
                        wait_full(dve, ("h2", u), i)
                        if u >= 3:
                            dve.wait_ge(l3_done, i * WIN + (u - 3) // 2 + 1)
                        freed(dve.tensor_scalar(H2[:, u % 3], slot(("h2", u)), B2[:, 0:1], 0.0, ALU.add, ALU.max), ("h2", u))

                wait_full(dve, ("bt", 0), i)
                for g in range(2):
                    src = slot(("bt", 0))[64 * g:64 * g + 64, 0:512].rearrange("p (t j u) -> p u t j", j=4, u=32)
                    for w in range(2):
                        ins = dve.tensor_copy(BS[64 * w:64 * w + 64, :, :, 4 * g:4 * g + 4], src[:, w:WIN:2])
                freed(ins, ("bt", 0))
                wait_emptied(dve, ("bt", 0), i)
                sm = SM[:].rearrange("p a (g j) -> p (a g) j", j=4)
                link(dve.tensor_tensor(SM[:], SM[:], BS.rearrange("p b t e -> p (b t) e"), ALU.add))
                link(dve.tensor_reduce(SMX[:], sm, AX.X, ALU.max))
                dve.tensor_tensor(sm, sm, SMX[:].unsqueeze(2).broadcast_to([P, 64, 4]), ALU.subtract).then_inc(sm_in, 1)
                dve.wait_ge(sm_exp, i + 1)
                link(dve.tensor_reduce(SMS[:], sm, AX.X, ALU.add))
                link(dve.reciprocal(SMS[:], SMS[:]))
                dve.wait_ge(az_zero, i + 1)
                for w in range(2):
                    rows = slice(64 * w, 64 * w + 64)
                    dve.tensor_tensor(az_window(w), SM[rows].rearrange("p (b t) (g j) -> p b (t g) j", b=PXT, g=2),
                                      SMS[rows].rearrange("p (b g) -> p b g", b=PXT).unsqueeze(3)
                                      .broadcast_to([64, PXT, 8, 4]), ALU.mult).then_inc(az_done, 1)
                for t in (1, 3):
                    wait_full(dve, ("at", t), i)
                    for a in range(4):
                        ins = dve.tensor_copy(raster(A[:, t])[:, a], windowed(slot(("at", t)))[:, a])
                    freed(ins, ("at", t))
                for t in (1, 3):
                    wait_full(dve, ("av", t), i)
                    freed(dve.tensor_copy(OL[:, t], slot(("av", t))), ("av", t))
                for t in range(CT):
                    wait_full(dve, ("o1", t), i)
                    if t >= 2:
                        dve.wait_ge(y_out[t % 2], i * 32 + 32)
                    freed(dve.scalar_tensor_tensor(out=YS[:, t % 2], in0=slot(("o1", t)), scalar=BO1[:, t:t + 1],
                                                   in1=X[:, t], op0=ALU.add, op1=ALU.add), ("o1", t))
                assert n_steps[0] == DVE_STEPS, n_steps[0]


N_LOADS = 22 + 9


def windowed(ap):
    return ap.rearrange("p (a b y x) -> p a y b x", a=4, b=4, y=8)


def raster(ap):
    return ap.rearrange("p (a y b x) -> p a y b x", a=4, y=8, b=4)


def kernel(**inputs):
    import numpy as np
    import concourse.bacc as bacc
    from concourse.bass_utils import run_bass_kernel_spmd

    f = {k: np.ascontiguousarray(v) for k, v in inputs.items()}

    def tiles(a):
        return np.ascontiguousarray(a.reshape(-1, P).T)

    part = np.arange(P)
    group = (part[:, None] // 16 == part[None, :] // 16).astype(np.float32) / 16
    pt = np.arange(64) % PTS
    gxy = np.tile(np.stack([pt % 2, pt // 2], 1), (1, 8)).astype(np.float32)
    px = np.arange(8, dtype=np.float32)
    grid = np.concatenate([px, np.float32(2.0) * px / np.float32(7) - np.float32(1.0)])
    grid = np.ascontiguousarray(np.broadcast_to(grid, (64, 16)))
    bqkv = f["L0_conv_bqkv"]
    arrays = {
        "x": f["x"].reshape(B, C, HW),
        "wqkv": f["L0_conv_Wqkv"],
        "bqk": tiles(bqkv[:2 * C]),
        "bv": np.ascontiguousarray(bqkv[2 * C:]),
        "wo0": f["L0_conv_Wout"],
        "bo0": tiles(f["L0_conv_bout"]),
        "lnw": f["L1_conv_ln_w"],
        "lnb": f["L1_conv_ln_b"],
        "wqT": np.ascontiguousarray(f["L1_conv_wq"].transpose(0, 2, 1)),
        "wkT": np.ascontiguousarray(f["L1_conv_wk"].transpose(0, 2, 1)),
        "wvT": np.ascontiguousarray(f["L1_conv_wv"].transpose(0, 2, 1)),
        "woT": np.ascontiguousarray(f["L1_conv_w_out"].T),
        "bo1": tiles(f["L1_conv_b_out"]),
        "dww": f["L1_conv_off_dw_w"].reshape(64, 36),
        "dwb": f["L1_conv_off_dw_b"].reshape(64, 1),
        "pwT": np.ascontiguousarray(f["L1_conv_off_pw_w"].T),
        "w1T": np.ascontiguousarray(f["L1_conv_cpb_w1"].T),
        "b1": f["L1_conv_cpb_b1"].reshape(1, P),
        "w2T": np.ascontiguousarray(f["L1_conv_cpb_w2"].T),
        "b2": f["L1_conv_cpb_b2"].reshape(P, 1),
        "w3c": np.ascontiguousarray(f["L1_conv_cpb_w3"].T),
        "b3": f["L1_conv_cpb_b3"],
        "c_ident": np.eye(P, dtype=np.float32),
        "c_gavg": group,
        "c_gxy": gxy,
        "c_grid": grid,
    }
    nc = bacc.Bacc("TRN2", target_bir_lowering=False, num_devices=1, dynamic_dma_scratch_size=1024)
    args = {n: nc.dram_tensor(f"in_{n}", a.shape, F32, kind="ExternalInput").ap() for n, a in arrays.items()}
    args["out"] = nc.dram_tensor("out", (B, C, HW), F32, kind="ExternalOutput").ap()
    build(nc, **args)
    r = run_bass_kernel_spmd(nc, [{f"in_{n}": a for n, a in arrays.items()}], core_ids=[0])
    return r.results[0]["out"].reshape(B, C, 32, 32)
```
